# Optimizing a Trainium2 kernel written in Bass

```python
import numpy as np
import jax
import jax.numpy as jnp

def _softmax(x, axis=-1):
    return jax.nn.softmax(x, axis=axis)

def _gelu(x):
    return jax.nn.gelu(x, approximate=True)

def _silu(x):
    return jax.nn.silu(x)

def _sigmoid(x):
    return jax.nn.sigmoid(x)

def _layernorm(x, axis=-1, eps=1e-05):
    m = jnp.mean(x, axis=axis, keepdims=True)
    v = jnp.var(x, axis=axis, keepdims=True)
    return (x - m) / jnp.sqrt(v + eps)

def _scatter_add(tgt, idx, src, axis=0):
    return tgt.at[idx].add(src)

def _segment_sum(src, seg, n):
    return jax.ops.segment_sum(src, seg, n)
kernel_name = 'mk_adaln_ffn_d1_seqx_r4_deb638'

def setup_inputs(seed: int=0):
    np.random.seed(seed)
    _w = jnp.asarray

    def _rec_inputs():
        import jax
        import jax.numpy as jnp
        _rk = jax.random.key(seed)
        x = -7.109e-05 + 0.9999 * jax.random.normal(jax.random.fold_in(_rk, 1), (128, 64, 1024), jnp.float32)
        _lenS = 64 - jax.random.randint(jax.random.fold_in(_rk, 7), (128,), 0, max(1, 64 // 4) + 1, jnp.int32)
        _lenS2 = 64 - jax.random.randint(jax.random.fold_in(_rk, 8), (128,), 0, max(1, 64 // 4) + 1, jnp.int32)
        itok_B_0_15 = jax.random.randint(jax.random.fold_in(_rk, 11), (128,), 0, 16, jnp.int32)
        return (x, itok_B_0_15)
    x, itok_B_0_15 = _rec_inputs()

    def _L0_cond_setup():
        import jax, jax.numpy as jnp
        import numpy as np
        MAX_LORAS = 16
        IN, OUT = (1024, 1024)
        B, S = (8, 512)
        key = jax.random.key(seed)
        k1, k2, k3 = jax.random.split(key, 3)
        x = jax.random.normal(k1, (B, S, IN), dtype=jnp.float32)
        adapter_ids = jax.random.randint(k2, (B,), 0, MAX_LORAS)
        weight = jax.random.normal(k3, (MAX_LORAS, OUT, IN), dtype=jnp.float32) * 0.02
        return {'x': x, 'adapter_ids': adapter_ids, 'weight': weight}
    _L0_cond_all = _L0_cond_setup()
    _L0_cond_in = {k: v for k, v in _L0_cond_all.items() if k in ('weight',)}
    del _L0_cond_all

    def _L0_ffn_setup():
        import jax, jax.numpy as jnp
        import numpy as np
        B_, S, D_IN, D_OUT = (4, 512, 1024, 1024)
        N, RANK, ALPHA = (8, 16, 32)
        SCALE = ALPHA / RANK
        key = jax.random.key(seed)
        kx, ka, kb, kw, kbias = jax.random.split(key, 5)
        x = jax.random.normal(kx, (B_, S, D_IN), dtype=jnp.float32)
        lora_A = jax.random.normal(ka, (N, RANK, D_IN), dtype=jnp.float32) * (1.0 / np.sqrt(D_IN))
        lora_B = jax.random.normal(kb, (N, D_OUT, RANK), dtype=jnp.float32) * (1.0 / np.sqrt(RANK))
        W = jax.random.normal(kw, (D_OUT, D_IN), dtype=jnp.float32) * (1.0 / np.sqrt(D_IN))
        bias = jax.random.normal(kbias, (D_OUT,), dtype=jnp.float32) * 0.01
        lora_weights = jnp.full((N,), 1.0 / N, dtype=jnp.float32)
        return {'x': x, 'lora_A': lora_A, 'lora_B': lora_B, 'W': W, 'bias': bias, 'lora_weights': lora_weights}
    _L0_ffn_all = _L0_ffn_setup()
    _L0_ffn_in = {k: v for k, v in _L0_ffn_all.items() if k in ('lora_A', 'lora_B', 'W', 'bias', 'lora_weights')}
    del _L0_ffn_all
    return {'x': x, 'itok_B_0_15': itok_B_0_15, 'L0_cond_weight': _L0_cond_in['weight'], 'L0_ffn_lora_A': _L0_ffn_in['lora_A'], 'L0_ffn_lora_B': _L0_ffn_in['lora_B'], 'L0_ffn_W': _L0_ffn_in['W'], 'L0_ffn_bias': _L0_ffn_in['bias'], 'L0_ffn_lora_weights': _L0_ffn_in['lora_weights']}

def reference(x, itok_B_0_15, L0_cond_weight, L0_ffn_lora_A, L0_ffn_lora_B, L0_ffn_W, L0_ffn_bias, L0_ffn_lora_weights):
    import jax
    import jax.numpy as jnp

    def _L0_cond_ref(x, adapter_ids, weight):
        import jax, jax.numpy as jnp
        import numpy as np
        MAX_LORAS = 16
        IN, OUT = (1024, 1024)
        B, S = (8, 512)
        w = weight[adapter_ids]
        return jnp.einsum('bsi,boi->bso', x, w)

    def _L0_ffn_ref(x, lora_A, lora_B, W, bias, lora_weights):
        import jax, jax.numpy as jnp
        import numpy as np
        B_, S, D_IN, D_OUT = (4, 512, 1024, 1024)
        N, RANK, ALPHA = (8, 16, 32)
        SCALE = ALPHA / RANK
        h = jnp.einsum('bsd,nrd->nbsr', x, lora_A)
        coef = (SCALE * lora_weights)[:, None, None]
        lora_out = jnp.einsum('nbsr,nor->bso', h, lora_B * coef)
        base = jnp.einsum('bsd,od->bso', x, W) + bias
        return base + lora_out
    x = x + _L0_ffn_ref(_L0_cond_ref(x, itok_B_0_15, L0_cond_weight), L0_ffn_lora_A, L0_ffn_lora_B, L0_ffn_W, L0_ffn_bias, L0_ffn_lora_weights)
    return x

_drawn_inputs = setup_inputs


def setup_inputs(seed=0):
    import zlib

    import numpy as np

    out = dict(_drawn_inputs(seed))
    spreads = {'L0_ffn_lora_weights': (0.125, 0.2)}
    factors = {'L0_ffn_bias': 7.464}
    for name, (base, spread) in spreads.items():
        noise = np.random.default_rng([zlib.crc32(name.encode()), seed]).standard_normal(out[name].shape)
        drawn = base * np.exp(spread * noise) if base else spread * noise
        out[name] = jnp.asarray(drawn.astype(out[name].dtype))
    for name, factor in factors.items():
        out[name] = (out[name] * factor).astype(out[name].dtype)
    return out
```

```python
import concourse.bass as bass
from concourse import mybir
from concourse.alu_op_type import AluOpType as ALU
from contextlib import ExitStack



def grouped_adaln_ffn_kernel(nc, x, ids, w, lora_a, lora_b, base_w, bias, lora_weights, out):
    f32, f32r, i32 = mybir.dt.float32, mybir.dt.float32r, mybir.dt.int32
    COPY = mybir.ActivationFunctionType.Copy
    AXX = mybir.AxisListType.X

    SAMPLES, TOK, D = x.shape
    EXPERTS = w.shape[0]
    NLORA, RANK, _ = lora_a.shape
    LORA_SCALE = 32 / RANK
    P = 128
    QUADS, BLK = 4, 32
    SEG = D // QUADS
    KT = D // P
    HALF = 512
    SLOTS = (SAMPLES + EXPERTS) // 2
    TILES = SAMPLES // 2
    POS = 2 * SLOTS
    CHUNKS = D // P
    RAW, TURN = 4, 2
    RING = 4
    AHEAD = 3
    FOLDS = D // P
    assert NLORA * RANK == P and 2 * TOK == P and SLOTS % RING == 0 and TILES % RING == 0

    ctx = ExitStack()
    with ctx:
        def sb(name, shape, dt):
            return ctx.enter_context(nc.sbuf_tensor(name, shape, dt))

        def sem(name):
            return ctx.enter_context(nc.semaphore(name))

        weff = nc.dram_tensor("weff", [D, D], f32, kind="Internal").ap()
        y_scr = nc.dram_tensor("y_scr", [POS, TOK, D], f32, kind="Internal").ap()

        EXPERT_BYTES = KT * D * 4
        base = -(-nc.sbuf_base // 64) * 64
        arena = sb("arena", [P, (4 * EXPERT_BYTES + base - nc.sbuf_base) // 4], f32)
        w_hi = nc.alloc_sbuf_tensor_at("w_hi", [P, 2, KT, D], f32r, offset=base)
        w_lo = nc.alloc_sbuf_tensor_at("w_lo", [P, 2, KT, D], f32r, offset=base + 2 * EXPERT_BYTES)
        fold_w = nc.alloc_sbuf_tensor_at("fold_w", [P, FOLDS, D], f32, offset=base + EXPERT_BYTES)
        spare = base + 3 * EXPERT_BYTES
        a_sb = nc.alloc_sbuf_tensor_at("a_sb", [P, D], f32, offset=spare)
        b_sb = nc.alloc_sbuf_tensor_at("b_sb", [P, FOLDS, NLORA, RANK], f32, offset=spare + 4 * D)
        bt_sb = nc.alloc_sbuf_tensor_at("bt_sb", [P, D], f32, offset=spare + 8 * D)

        w_raw = [sb(f"w_raw{b}", [P, P // BLK, SEG], f32) for b in range(RAW)]
        w_turn = [sb(f"w_turn{b}", [P, KT, P], f32) for b in range(TURN)]
        x_raw = [sb(f"x_raw{b}", [P, P // BLK, SEG], f32) for b in range(2)]
        x_turn = [sb(f"x_turn{h}", [P, KT // 2, P], f32) for h in range(2)]
        x_hi = [sb(f"x_hi{b}", [P, KT, P], f32r) for b in range(RING)]
        x_lo = [sb(f"x_lo{b}", [P, KT, P], f32r) for b in range(RING)]
        stage = [sb(f"stage{b}", [P, D], f32) for b in range(2)]
        bias_sb = w_raw[0]

        spare_at = [spare + 12 * D]

        def scratch(name, shape, dt):
            n = 4
            for k in shape[1:]:
                n *= k
            at = spare_at[0]
            spare_at[0] += -(-n // 64) * 64
            assert spare_at[0] <= spare + EXPERT_BYTES
            return nc.alloc_sbuf_tensor_at(name, shape, dt, offset=at)

        ids_i = scratch("ids_i", [P, 1], i32)
        ids_f = scratch("ids_f", [P, 1], f32)
        iota_i = scratch("iota_i", [P, POS], i32)
        iota_f = scratch("iota_f", [P, POS], f32)
        chan_i = scratch("chan_i", [P, 1], i32)
        chan_f = scratch("chan_f", [P, 1], f32)
        onehot = scratch("onehot", [P, EXPERTS], f32)
        ones = scratch("ones", [P, P], f32)
        before = scratch("before", [P, P], f32)
        ident = scratch("ident", [P, P], f32)
        counts = scratch("counts", [P, 4, EXPERTS], f32)
        halves_i = scratch("halves_i", [P, EXPERTS], i32)
        scan = scratch("scan", [P, 2, 3, EXPERTS], f32)
        picked = scratch("picked", [P, 4, EXPERTS], f32)
        mine = scratch("mine", [P, 4], f32)
        vals = scratch("vals", [P, 6], f32)
        at_pos = scratch("at_pos", [P, POS], f32)
        at_order = scratch("at_order", [P, SAMPLES], f32)
        at_rank = scratch("at_rank", [P, EXPERTS + 1], f32)
        slot_sample = sb("slot_sample", [1, POS], i32)
        slot_rank = sb("slot_rank", [1, POS], i32)
        slot_opens = sb("slot_opens", [1, POS], i32)
        slot_used = sb("slot_used", [1, POS], i32)
        order_sample = sb("order_sample", [1, SAMPLES], i32)
        order_pos = sb("order_pos", [1, SAMPLES], i32)
        rank_expert = sb("rank_expert", [1, EXPERTS + 1], i32)
        n_ranks = sb("n_ranks", [1, 1], i32)
        coef = sb("coef", [P, 1], f32)

        ps = [ctx.enter_context(nc.psum_tensor(f"ps{b}", [P, D], f32)) for b in range(RING)]

        ids_loaded = sem("ids_loaded")
        lora_loaded = sem("lora_loaded")
        base_loaded = sem("base_loaded")
        iotas = sem("iotas")
        routing = sem("routing")
        counted = sem("counted")
        listed = sem("listed")
        tables = sem("tables")
        b_turned = sem("b_turned")
        b_scaled = sem("b_scaled")
        fold_added = sem("fold_added")
        w_loaded = [sem(f"w_loaded{b}") for b in range(RAW)]
        w_turned = sem("w_turned")
        w_rounded = sem("w_rounded")
        w_ready = sem("w_ready")
        x_loaded = [sem(f"x_loaded{b}") for b in range(2)]
        x_turned = sem("x_turned")
        x_rounded = sem("x_rounded")
        x_ready = sem("x_ready")
        tile_done = sem("tile_done")
        moved = sem("moved")
        stored = [sem(f"stored{b}") for b in range(2)]
        bias_loaded = sem("bias_loaded")
        rest_loaded = [sem(f"rest_loaded{b}") for b in range(2)]
        rest_biased = sem("rest_biased")
        out_added = sem("out_added")
        out_stored = [sem(f"out_stored{b}") for b in range(2)]

        route_steps = []

        block = ctx.enter_context(nc.Block())

        def entry(eng, table, i, top):
            return eng.value_load(table[0:1, bass.ds(i, 1)], min_val=0, max_val=top)

        @block.sync
        def _(sp):
            def load_expert(k, src):
                for c in range(CHUNKS):
                    if not (isinstance(k, int) and k == 0 and c < RAW):
                        sp.wait_ge(w_turned, k * CHUNKS + (c - RAW + 1))
                    rows = src[c * P:(c + 1) * P, :].rearrange("(m j) n -> j m n", j=BLK)
                    for q in range(QUADS):
                        sp.dma_start(w_raw[c % RAW][BLK * q:BLK * (q + 1), :, :],
                                     rows[:, :, q * SEG:(q + 1) * SEG]).then_inc(w_loaded[c % RAW], 16)

            def load_two(buf, loaded, first, second):
                for h, rows in enumerate((first, second)):
                    view = rows.rearrange("(m j) n -> j m n", j=BLK)
                    for q in range(QUADS):
                        sp.dma_start(buf[BLK * q:BLK * (q + 1), 2 * h:2 * h + 2, :],
                                     view[:, :, q * SEG:(q + 1) * SEG]).then_inc(loaded, 16)

            def one(tensor, i):
                return tensor[bass.ds(i, 1)].rearrange("a s n -> (a s) n")

            def load_x(n, b):
                if not (isinstance(n, int) and n < 2):
                    sp.wait_ge(x_turned, 2 * n - 2)
                s0 = entry(sp, slot_sample, 2 * n, SAMPLES - 1)
                s1 = entry(sp, slot_sample, 2 * n + 1, SAMPLES - 1)
                load_two(x_raw[b], x_loaded[b], one(x, s0), one(x, s1))

            def load_y(t, group, u):
                b = (SLOTS + u) % 2
                p0 = entry(sp, order_pos, 2 * t, POS - 1)
                p1 = entry(sp, order_pos, 2 * t + 1, POS - 1)
                last = [u + EXPERTS // 2 - (p if isinstance(group, int) else 0) for p in range(2)]
                stores = [sp.snap(group * (16 * RING // 2) + 16 * (FOLDS // 2 + last[p] // 2 + 1)) for p in range(2)]
                turned = sp.snap(2 * (t + SLOTS) - 2)
                for p in range(2):
                    sp.wait_ge(stored[p], stores[p])
                sp.wait_ge(x_turned, turned)
                load_two(x_raw[b], x_loaded[b], one(y_scr, p0), one(y_scr, p1))

            def load_rest(t, b, stores=None):
                samples = [entry(sp, order_sample, 2 * t + h, SAMPLES - 1) for h in range(2)]
                if stores is not None:
                    sp.wait_ge(out_stored[b], stores)
                for h in range(2):
                    sp.dma_start(stage[b][h * TOK:(h + 1) * TOK, :], one(x, samples[h])).then_inc(rest_loaded[b], 16)

            def load_next_expert(slot):
                opens = entry(sp, slot_opens, 2 * slot, 1)
                with sp.If(opens > 0):
                    rank = entry(sp, slot_rank, 2 * slot, EXPERTS - 1)
                    load_rank(rank + 1)
                with sp.Else():
                    sp.nop()

            def load_rank(k):
                e = entry(sp, rank_expert, k, EXPERTS)
                with sp.If(e < EXPERTS):
                    load_expert(k, one(w, entry(sp, rank_expert, k, EXPERTS - 1)))
                with sp.Else():
                    load_expert(k, weff)
                sp.nop()

            sp.dma_start(ids_i[:, :], ids.rearrange("(s a) -> s a", a=1)).then_inc(ids_loaded, 16)
            load_expert(0, w[0])
            sp.wait_ge(tables, 1)
            for n in range(AHEAD):
                load_x(n, n % 2)
            for p in range(2):
                sp.wait_ge(stored[p], 16 * (FOLDS // 2))
            load_rank(1)
            with sp.Fori(0, SLOTS // RING - 1) as g:
                for u in range(RING):
                    load_x(g * RING + (u + AHEAD), (u + AHEAD) % 2)
                    load_next_expert(g * RING + u)
            for u in range(RING):
                slot = SLOTS - RING + u
                if u + AHEAD < RING:
                    load_x(slot + AHEAD, (u + AHEAD) % 2)
                else:
                    load_y(u + AHEAD - RING, 0, u + AHEAD - RING)
                load_next_expert(slot)
            ranks = entry(sp, n_ranks, 0, EXPERTS)
            sp.wait_ge(w_turned, ranks * CHUNKS + CHUNKS)
            sp.dma_start(bias_sb[:, :, :].rearrange("p m n -> p (m n)"),
                         bias.rearrange("(a n) -> a n", a=1).to_broadcast([P, D])).then_inc(bias_loaded, 16)
            for t in range(2):
                sp.wait_ge(stored[t], 16 * (FOLDS // 2 + SLOTS // 2))
                load_rest(t, t)

            def out_step(g, u, last):
                t = g * RING + u
                if not (last and u + AHEAD >= RING):
                    v = u + AHEAD
                    load_y(t + AHEAD, g + v // RING, v % RING)
                if not (last and u + 2 >= RING):
                    load_rest(t + 2, u % 2, g * (32 * RING // 2) + 32 * (u // 2 + 1))

            with sp.Fori(0, TILES // RING - 1) as g:
                for u in range(RING):
                    out_step(g, u, False)
            for u in range(RING):
                out_step(TILES // RING - 1, u, True)
            for b in range(2):
                sp.wait_ge(out_stored[b], 32 * TILES // 2)

        @block.gpsimd
        def _(pool):
            nc.gpsimd.iota(iota_i[:, :], [[1, POS]], base=0, channel_multiplier=0).then_inc(iotas, 1)
            nc.gpsimd.iota(chan_i[:, :], [[0, 1]], base=0, channel_multiplier=1).then_inc(iotas, 1)
            pool.wait_ge(base_loaded, 16)
            for f in range(FOLDS):
                pool.wait_ge(moved, f + 1)
                nc.gpsimd.tensor_tensor(fold_w[:, f, :], fold_w[:, f, :], stage[f % 2][:, :],
                                        ALU.add).then_inc(fold_added, 1)
            pool.wait_ge(bias_loaded, 16)
            with pool.Fori(0, TILES // 2) as g:
                for b in range(2):
                    pool.wait_ge(rest_loaded[b], g * 32 + 32)
                    nc.gpsimd.tensor_tensor(stage[b][:, :], stage[b][:, :],
                                            bias_sb[:, :, :].rearrange("p m n -> p (m n)"),
                                            ALU.add).then_inc(rest_biased, 1)

        @block.scalar
        def _(act):
            for n in range(NLORA):
                act.dma_start(b_sb[:, :, n, :], lora_b[n].rearrange("(f p) r -> p f r", p=P)).then_inc(lora_loaded, 16)
            act.dma_start(a_sb[:, :], lora_a.rearrange("n r d -> (n r) d")).then_inc(lora_loaded, 16)
            for n in range(NLORA):
                act.dma_start(coef[n * RANK:(n + 1) * RANK, :],
                              lora_weights[n:n + 1].rearrange("(a b) -> a b", a=1).to_broadcast([RANK, 1])
                              ).then_inc(lora_loaded, 16)
            act.dma_start(fold_w[:, :, :], base_w.rearrange("(f p) n -> p f n", p=P)).then_inc(base_loaded, 16)

            def round_w(k, par):
                for c in range(CHUNKS):
                    act.wait_ge(w_turned, k * CHUNKS + (c + 1))
                    dst = w_hi[:, bass.ds(par, 1), :, c * P:(c + 1) * P].rearrange("p a t m -> p (a t) m")
                    nc.scalar.activation(dst, w_turn[c % TURN][:, :, :], COPY).then_inc(w_rounded, 1)

            def round_x(n, b):
                if not (isinstance(n, int) and n < RING):
                    act.wait_ge(tile_done, n + (FOLDS - RING + 1))
                for h in range(2):
                    act.wait_ge(x_turned, 2 * n + (h + 1))
                    nc.scalar.activation(x_hi[b][:, h * KT // 2:(h + 1) * KT // 2, :],
                                         x_turn[h][:, :, :], COPY).then_inc(x_rounded, 1)

            def round_next_expert(slot):
                opens = entry(act, slot_opens, 2 * slot, 1)
                with act.If(opens > 0):
                    rank = entry(act, slot_rank, 2 * slot, EXPERTS - 1)
                    act.wait_ge(tile_done, slot + FOLDS)
                    round_w(rank + 1, (rank + 1) % 2)
                with act.Else():
                    act.nop()

            def move_y(slot, u, g):
                act.wait_ge(tile_done, slot + (FOLDS + 1))
                act.wait_ge(stored[u % 2], g * (16 * RING // 2) + 16 * (FOLDS // 2 + u // 2))
                nc.scalar.activation(stage[u % 2][:, :], ps[u][:, :], COPY).then_inc(moved, 1)
                act.wait_ge(moved, slot + (FOLDS + 1))
                act.dma_start(y_scr[bass.ds(2 * slot, 2)].rearrange("a s n -> (a s) n"),
                              stage[u % 2][:, :]).then_inc(stored[u % 2], 16)

            round_w(0, 0)
            act.wait_ge(tables, 1)
            for n in range(AHEAD):
                round_x(n, n)

            def store_fold(f):
                act.wait_ge(fold_added, f + 1)
                act.dma_start(weff[f * P:(f + 1) * P, :], fold_w[:, f, :]).then_inc(stored[f % 2], 16)

            for f in range(FOLDS):
                act.wait_ge(tile_done, f + 1)
                if f >= 2:
                    act.wait_ge(fold_added, f - 1)
                nc.scalar.activation(stage[f % 2][:, :], ps[f % RING][:, :], COPY).then_inc(moved, 1)
                if f >= 1:
                    store_fold(f - 1)
            store_fold(FOLDS - 1)
            for p in range(2):
                act.wait_ge(stored[p], 16 * (FOLDS // 2))
            round_w(1, 1)
            with act.Fori(0, SLOTS // RING) as g:
                for u in range(RING):
                    slot = g * RING + u
                    round_x(slot + AHEAD, (u + AHEAD) % RING)
                    round_next_expert(slot)
                    move_y(slot, u, g)

            def out_step(g, u, last):
                t = g * RING + u
                if not (last and u + AHEAD >= RING):
                    round_x(t + (SLOTS + AHEAD), (u + AHEAD) % RING)
                act.wait_ge(out_added, t + 1)
                for h in range(2):
                    s = entry(act, order_sample, 2 * t + h, SAMPLES - 1)
                    act.dma_start(out[bass.ds(s, 1)].rearrange("a s n -> (a s) n"),
                                  stage[u % 2][h * TOK:(h + 1) * TOK, :]).then_inc(out_stored[u % 2], 16)

            with act.Fori(0, TILES // RING - 1) as g:
                for u in range(RING):
                    out_step(g, u, False)
            for u in range(RING):
                out_step(TILES // RING - 1, u, True)

        @block.vector
        def _(dve):
            step = [0]

            def link(ins):
                step[0] += 1
                ins.then_inc(routing, 1)
                dve.wait_ge(routing, step[0])

            tt, tsc, cp = nc.vector.tensor_tensor, nc.vector.tensor_scalar, nc.vector.tensor_copy

            link(nc.vector.memset(ones[:, :], 1.0))
            dve.wait_ge(iotas, 2)
            link(cp(iota_f[:, :], iota_i[:, :]))
            link(cp(chan_f[:, :], chan_i[:, :]))
            dve.wait_ge(ids_loaded, 16)
            link(cp(ids_f[:, :], ids_i[:, :]))
            link(tsc(before[:, :], iota_f[:, 0:P], chan_f[:, 0:1], None, ALU.is_gt))
            link(tsc(ident[:, :], iota_f[:, 0:P], chan_f[:, 0:1], None, ALU.is_equal))
            link(tsc(onehot[:, :], iota_f[:, 0:EXPERTS], ids_f[:, 0:1], None, ALU.is_equal))
            onehot_step = step[0]
            dve.wait_ge(counted, 1)
            link(cp(counts[:, 2, :], ps[0][:, 0:EXPERTS]))
            link(cp(counts[:, 3, :], ps[0][:, EXPERTS:2 * EXPERTS]))
            link(tsc(counts[:, 1, :], counts[:, 2, :], 0.0, None, ALU.is_gt))
            link(nc.vector.memset(counts[:, 1, 0:1], 1.0))
            link(tsc(halves_i[:, :], counts[:, 2, :], 1.0, None, ALU.add))
            link(tsc(halves_i[:, :], halves_i[:, :], 1, None, ALU.arith_shift_right))
            link(cp(counts[:, 0, :], halves_i[:, :]))
            link(cp(scan[:, 0, :, :], counts[:, 0:3, :]))
            src, d = 0, 1
            while d < EXPERTS:
                link(cp(scan[:, 1 - src, :, 0:d], scan[:, src, :, 0:d]))
                link(tt(scan[:, 1 - src, :, d:], scan[:, src, :, d:], scan[:, src, :, :EXPERTS - d], ALU.add))
                src, d = 1 - src, 2 * d
            link(cp(n_ranks[0:1, :], scan[0:1, src, 1, EXPERTS - 1:EXPERTS]))
            link(tt(counts[:, 0:3, :], scan[:, src, :, :], counts[:, 0:3, :], ALU.subtract))
            for i in range(4):
                link(tt(picked[:, i, :], counts[:, i, :], onehot[:, :], ALU.mult))
            link(nc.vector.reduce_sum(mine[:, :], picked[:, :, :], AXX))
            link(cp(vals[:, 0:1], chan_f[:, :]))
            link(cp(vals[:, 1:2], mine[:, 1:2]))
            link(nc.vector.memset(vals[:, 3:4], 1.0))
            link(tsc(vals[:, 4:5], mine[:, 0:1], 2.0, mine[:, 3:4], ALU.mult, ALU.add))
            order = picked[:, 0, 0:1]
            link(tt(order, mine[:, 2:3], mine[:, 3:4], ALU.add))
            leads = picked[:, 1, 0:1]
            link(tsc(leads, mine[:, 3:4], 0.0, None, ALU.is_equal))
            link(tsc(vals[:, 2:3], mine[:, 1:2], 0.5, leads, ALU.is_gt, ALU.mult))
            link(tsc(vals[:, 5:6], ids_f[:, :], float(-EXPERTS), leads, ALU.add, ALU.mult))
            link(tsc(at_pos[:, :], iota_f[:, 0:POS], vals[:, 4:5], None, ALU.is_equal))
            link(tsc(at_order[:, :], iota_f[:, 0:SAMPLES], order, None, ALU.is_equal))
            link(tsc(at_rank[:, :], iota_f[:, 0:EXPERTS + 1], mine[:, 1:2], None, ALU.is_equal))
            listed_step = step[0]
            dve.wait_ge(listed, 1)
            link(cp(slot_sample[:, :], ps[1][0:1, 0:POS]))
            link(cp(slot_rank[:, :], ps[1][0:1, POS:2 * POS]))
            link(cp(slot_opens[:, :], ps[1][0:1, 2 * POS:3 * POS]))
            link(cp(slot_used[:, :], ps[1][0:1, HALF:HALF + POS]))
            link(cp(order_sample[:, :], ps[1][0:1, HALF + POS:HALF + POS + SAMPLES]))
            link(cp(order_pos[:, :], ps[1][0:1, HALF + POS + SAMPLES:HALF + POS + 2 * SAMPLES]))
            link(tsc(rank_expert[:, :], ps[2][0:1, 0:EXPERTS + 1], float(EXPERTS), None, ALU.add))
            nc.vector.memset(counts[:, 0, 0:1], 0.0).then_inc(tables, 1)

            def turn_w(k, c):
                dve.wait_ge(w_loaded[c % RAW], 16 * QUADS * (c // RAW + 1) + k * (16 * QUADS * CHUNKS // RAW))
                if not (isinstance(k, int) and k == 0 and c < TURN):
                    dve.wait_ge(w_ready, k * CHUNKS + (c - TURN + 1))
                nc.vector.transpose(w_turn[c % TURN][:, :, :].rearrange("p t (m j) -> p m t j", j=BLK),
                                    w_raw[c % RAW][:, :, :].rearrange("p m (t i) -> p m t i", i=BLK)
                                    ).then_inc(w_turned, 1)

            def split_w(k, par, c):
                dve.wait_ge(w_rounded, k * CHUNKS + (c + 1))
                part = slice(c * P, (c + 1) * P)
                hi = w_hi[:, bass.ds(par, 1), :, part].rearrange("p a t m -> p (a t) m")
                lo = w_lo[:, bass.ds(par, 1), :, part].rearrange("p a t m -> p (a t) m")
                tt(lo, w_turn[c % TURN][:, :, :], hi, ALU.subtract).then_inc(w_ready, 1)

            def scale_b():
                dve.wait_ge(b_turned, 1)
                tsc(bt_sb[:, :], ps[3][:, :], coef[:, 0:1], LORA_SCALE, ALU.mult, ALU.mult).then_inc(b_scaled, 1)

            def prepare_w(k, par):
                for c in range(CHUNKS):
                    if isinstance(k, int) and k == 0 and c == CHUNKS // 2:
                        scale_b()
                    turn_w(k, c)
                    if c:
                        split_w(k, par, c - 1)
                split_w(k, par, CHUNKS - 1)

            def prepare_x(n, b, raw, load):
                dve.wait_ge(x_loaded[raw], load * 128 + 128)
                for h in range(2):
                    if not (isinstance(n, int) and n == 0):
                        dve.wait_ge(x_ready, 2 * n + (h - 1))
                    ts = slice(h * KT // 2 * BLK, (h + 1) * KT // 2 * BLK)
                    nc.vector.transpose(x_turn[h][:, :, :].rearrange("p t (m j) -> p m t j", j=BLK),
                                        x_raw[raw][:, :, ts].rearrange("p m (t i) -> p m t i", i=BLK)
                                        ).then_inc(x_turned, 1)
                for h in range(2):
                    dve.wait_ge(x_rounded, 2 * n + (h + 1))
                    ts = slice(h * KT // 2, (h + 1) * KT // 2)
                    tt(x_lo[b][:, ts, :], x_turn[h][:, :, :], x_hi[b][:, ts, :], ALU.subtract).then_inc(x_ready, 1)

            def prepare_next_expert(slot):
                opens = entry(dve, slot_opens, 2 * slot, 1)
                with dve.If(opens > 0):
                    rank = entry(dve, slot_rank, 2 * slot, EXPERTS - 1)
                    prepare_w(rank + 1, (rank + 1) % 2)
                with dve.Else():
                    dve.nop()

            prepare_w(0, 0)
            for n in range(AHEAD):
                prepare_x(n, n, n % 2, n // 2)
            prepare_w(1, 1)
            with dve.Fori(0, SLOTS // RING) as g:
                for u in range(RING):
                    slot = g * RING + u
                    v = u + AHEAD
                    prepare_x(slot + AHEAD, v % RING, v % 2, g * (RING // 2) + v // 2)
                    prepare_next_expert(slot)

            def out_step(g, u, last):
                t = g * RING + u
                v = u + AHEAD
                if not (last and v >= RING):
                    prepare_x(t + (SLOTS + AHEAD), v % RING, v % 2, g * (RING // 2) + (v // 2 + SLOTS // 2))
                dve.wait_ge(tile_done, t + (FOLDS + SLOTS + 1))
                dve.wait_ge(rest_biased, t + 1)
                tt(stage[u % 2][:, :], ps[u][:, :], stage[u % 2][:, :], ALU.add).then_inc(out_added, 1)

            with dve.Fori(0, TILES // RING - 1) as g:
                for u in range(RING):
                    out_step(g, u, False)
            for u in range(RING):
                out_step(TILES // RING - 1, u, True)
            route_steps[:] = [onehot_step, listed_step]

        @block.tensor
        def _(pe):
            mm = nc.tensor.matmul
            onehot_step, listed_step = route_steps
            pe.wait_ge(routing, onehot_step)
            mm(ps[0][:, 0:EXPERTS], ones[:, :], onehot[:, :], start=True, stop=True)
            mm(ps[0][:, EXPERTS:2 * EXPERTS], before[:, :], onehot[:, :], start=True, stop=True).then_inc(counted, 1)
            pe.wait_ge(routing, listed_step)
            mm(ps[1][0:1, 0:POS], vals[:, 0:1], at_pos[:, :], start=True, stop=True)
            mm(ps[1][0:1, POS:2 * POS], vals[:, 1:2], at_pos[:, :], start=True, stop=True)
            mm(ps[1][0:1, 2 * POS:3 * POS], vals[:, 2:3], at_pos[:, :], start=True, stop=True)
            mm(ps[1][0:1, HALF:HALF + POS], vals[:, 3:4], at_pos[:, :], start=True, stop=True)
            mm(ps[1][0:1, HALF + POS:HALF + POS + SAMPLES], vals[:, 0:1], at_order[:, :], start=True, stop=True)
            mm(ps[1][0:1, HALF + POS + SAMPLES:HALF + POS + 2 * SAMPLES], vals[:, 4:5], at_order[:, :],
               start=True, stop=True)
            mm(ps[2][0:1, 0:EXPERTS + 1], vals[:, 5:6], at_rank[:, :], start=True, stop=True).then_inc(listed, 1)
            pe.wait_ge(lora_loaded, 16 * (2 * NLORA + 1))
            for f in range(FOLDS):
                last = nc.tensor.transpose(ps[3][:, f * P:(f + 1) * P],
                                           b_sb[:, f, :, :].rearrange("p n r -> p (n r)"), ident[:, :])
            last.then_inc(b_turned, 1)
            pe.wait_ge(b_scaled, 1)
            pe.wait_ge(tables, 1)
            for f in range(FOLDS):
                if f >= RING:
                    pe.wait_ge(moved, f - RING + 1)
                for half in range(2):
                    cols = slice(half * HALF, (half + 1) * HALF)
                    last = mm(ps[f % RING][:, cols], bt_sb[:, f * P:(f + 1) * P], a_sb[:, cols],
                              start=True, stop=True)
                last.then_inc(tile_done, 1)

            def products(b, par, ready):
                for half in range(2):
                    pe.wait_ge(w_ready, ready + (half + 1) * CHUNKS // 2)
                    cols = slice(half * HALF, (half + 1) * HALF)
                    for t in range(KT):
                        hi = w_hi[:, bass.ds(par, 1), t, cols].rearrange("p a m -> p (a m)")
                        lo = w_lo[:, bass.ds(par, 1), t, cols].rearrange("p a m -> p (a m)")
                        mm(ps[b][:, cols], x_hi[b][:, t, :], hi, start=t == 0, stop=False)
                        mm(ps[b][:, cols], x_hi[b][:, t, :], lo, start=False, stop=False)
                        last = mm(ps[b][:, cols], x_lo[b][:, t, :], hi, start=False, stop=t == KT - 1)
                last.then_inc(tile_done, 1)

            with pe.Fori(0, SLOTS // RING) as g:
                for u in range(RING):
                    slot = g * RING + u
                    used = entry(pe, slot_used, 2 * slot, 1)
                    pe.wait_ge(x_ready, 2 * slot + 2)
                    pe.wait_ge(moved, slot + (FOLDS - RING + 1))
                    with pe.If(used > 0):
                        rank = entry(pe, slot_rank, 2 * slot, EXPERTS - 1)
                        products(u, rank % 2, rank * CHUNKS)
                    with pe.Else():
                        for half in range(2):
                            last = mm(ps[u][:, half * HALF:(half + 1) * HALF], x_hi[u][:, 0, :],
                                      x_hi[u][:, 0:KT // 2, :], start=True, stop=True)
                        last.then_inc(tile_done, 1)
            ranks = entry(pe, n_ranks, 0, EXPERTS)
            par = pe.snap(ranks % 2)
            ready = pe.snap(ranks * CHUNKS)
            for u in range(RING):
                pe.wait_ge(x_ready, 2 * (SLOTS + u) + 2)
                pe.wait_ge(moved, FOLDS + SLOTS - RING + u + 1)
                products(u, par, ready)
            with pe.Fori(1, TILES // RING) as g:
                for u in range(RING):
                    t = g * RING + u
                    pe.wait_ge(x_ready, 2 * t + (2 * SLOTS + 2))
                    pe.wait_ge(out_added, t - (RING - 1))
                    products(u, par, ready)


_INS = ['x', 'itok_B_0_15', 'L0_cond_weight', 'L0_ffn_lora_A', 'L0_ffn_lora_B', 'L0_ffn_W', 'L0_ffn_bias',
        'L0_ffn_lora_weights']
_OUTS = [((128, 64, 1024), 'float32')]


def kernel(**inputs):
    import numpy as _np
    import concourse.bacc as _bacc
    from concourse import mybir as _mybir
    from concourse.bass_utils import run_bass_kernel_spmd as _run

    nc = _bacc.Bacc("TRN2", target_bir_lowering=False, num_devices=1)
    arrays, args = {}, []
    for name in _INS:
        a = _np.ascontiguousarray(inputs[name])
        arrays[f"in_{name}_dram"] = a
        args.append(nc.dram_tensor(f"in_{name}_dram", a.shape, _mybir.dt.from_np(a.dtype), kind="ExternalInput").ap())
    for i, (shape, dtype) in enumerate(_OUTS):
        dt = _mybir.dt.from_np(_np.dtype(dtype))
        args.append(nc.dram_tensor(f"out_{i}_dram", shape, dt, kind="ExternalOutput").ap())
    grouped_adaln_ffn_kernel(nc, *args)
    r = _run(nc, [arrays], core_ids=[0])
    return r.results[0]["out_0_dram"]
```

```python
import concourse.bass as bass
from concourse import mybir
from concourse.alu_op_type import AluOpType as ALU
from contextlib import ExitStack



def grouped_adaln_ffn_kernel(nc, x, ids, w, lora_a, lora_b, base_w, bias, lora_weights, out):
    f32, f32r, i32 = mybir.dt.float32, mybir.dt.float32r, mybir.dt.int32
    COPY = mybir.ActivationFunctionType.Copy
    AXX = mybir.AxisListType.X

    SAMPLES, TOK, D = x.shape
    EXPERTS = w.shape[0]
    NLORA, RANK, _ = lora_a.shape
    LORA_SCALE = 32 / RANK
    P = 128
    QUADS, BLK = 4, 32
    SEG = D // QUADS
    KT = D // P
    HALF = 512
    SLOTS = (SAMPLES + EXPERTS) // 2
    TILES = SAMPLES // 2
    POS = 2 * SLOTS
    CHUNKS = D // P
    LOADS = CHUNKS // 2
    TURN = 2
    RING = 4
    AHEAD = 3
    FOLDS = D // P
    assert NLORA * RANK == P and 2 * TOK == P and SLOTS % RING == 0 and TILES % RING == 0

    ctx = ExitStack()
    with ctx:
        def sb(name, shape, dt):
            return ctx.enter_context(nc.sbuf_tensor(name, shape, dt))

        def sem(name):
            return ctx.enter_context(nc.semaphore(name))

        weff = nc.dram_tensor("weff", [D, D], f32, kind="Internal").ap()
        y_scr = nc.dram_tensor("y_scr", [POS, QUADS, TOK, SEG], f32, kind="Internal").ap()

        EXPERT_BYTES = KT * D * 4
        base = -(-nc.sbuf_base // 64) * 64
        arena = sb("arena", [P, (4 * EXPERT_BYTES + base - nc.sbuf_base) // 4], f32)
        w_hi = nc.alloc_sbuf_tensor_at("w_hi", [P, 2, KT, D], f32r, offset=base)
        w_lo = nc.alloc_sbuf_tensor_at("w_lo", [P, 2, KT, D], f32r, offset=base + 2 * EXPERT_BYTES)
        fold_w = nc.alloc_sbuf_tensor_at("fold_w", [P, FOLDS, D], f32, offset=base + EXPERT_BYTES)
        spare = base + 3 * EXPERT_BYTES
        a_sb = nc.alloc_sbuf_tensor_at("a_sb", [P, D], f32, offset=spare)
        b_sb = nc.alloc_sbuf_tensor_at("b_sb", [P, FOLDS, NLORA, RANK], f32, offset=spare + 4 * D)
        bt_sb = nc.alloc_sbuf_tensor_at("bt_sb", [P, D], f32, offset=spare + 8 * D)

        w_raw = [sb(f"w_raw{b}", [P, 2 * P // BLK, SEG], f32) for b in range(2)]
        w_turn = [sb(f"w_turn{b}", [P, KT, P], f32) for b in range(TURN)]
        x_raw = [sb(f"x_raw{b}", [P, P // BLK, SEG], f32) for b in range(2)]
        x_turn = [sb(f"x_turn{h}", [P, KT // 2, P], f32) for h in range(2)]
        x_hi = [sb(f"x_hi{b}", [P, KT, P], f32r) for b in range(RING)]
        x_lo = [sb(f"x_lo{b}", [P, KT, P], f32r) for b in range(RING)]
        stage = [sb(f"stage{b}", [P, D], f32) for b in range(2)]
        bias_sb = w_raw[0][:, 0:D // SEG, :].rearrange("p m n -> p (m n)")

        spare_at = [spare + 12 * D]

        def scratch(name, shape, dt):
            n = 4
            for k in shape[1:]:
                n *= k
            at = spare_at[0]
            spare_at[0] += -(-n // 64) * 64
            assert spare_at[0] <= spare + EXPERT_BYTES
            return nc.alloc_sbuf_tensor_at(name, shape, dt, offset=at)

        ids_i = scratch("ids_i", [P, 1], i32)
        ids_f = scratch("ids_f", [P, 1], f32)
        iota_i = scratch("iota_i", [P, POS], i32)
        iota_f = scratch("iota_f", [P, POS], f32)
        chan_i = scratch("chan_i", [P, 1], i32)
        chan_f = scratch("chan_f", [P, 1], f32)
        onehot = scratch("onehot", [P, EXPERTS], f32)
        ones = scratch("ones", [P, P], f32)
        before = scratch("before", [P, P], f32)
        ident = scratch("ident", [P, P], f32)
        counts = scratch("counts", [P, 4, EXPERTS], f32)
        halves_i = scratch("halves_i", [P, EXPERTS], i32)
        scan = scratch("scan", [P, 2, 3, EXPERTS], f32)
        picked = scratch("picked", [P, 4, EXPERTS], f32)
        mine = scratch("mine", [P, 4], f32)
        vals = scratch("vals", [P, 6], f32)
        at_pos = scratch("at_pos", [P, POS], f32)
        at_order = scratch("at_order", [P, SAMPLES], f32)
        at_rank = scratch("at_rank", [P, EXPERTS + 1], f32)
        slot_sample = sb("slot_sample", [1, POS], i32)
        slot_rank = sb("slot_rank", [1, POS], i32)
        slot_opens = sb("slot_opens", [1, POS], i32)
        slot_used = sb("slot_used", [1, POS], i32)
        order_sample = sb("order_sample", [1, SAMPLES], i32)
        order_pos = sb("order_pos", [1, SAMPLES], i32)
        rank_expert = sb("rank_expert", [1, EXPERTS + 1], i32)
        n_ranks = sb("n_ranks", [1, 1], i32)
        coef = sb("coef", [P, 1], f32)

        ps = [ctx.enter_context(nc.psum_tensor(f"ps{b}", [P, D], f32)) for b in range(RING)]

        ids_loaded = sem("ids_loaded")
        lora_loaded = sem("lora_loaded")
        base_loaded = sem("base_loaded")
        iotas = sem("iotas")
        routing = sem("routing")
        counted = sem("counted")
        listed = sem("listed")
        tables = sem("tables")
        b_turned = sem("b_turned")
        b_scaled = sem("b_scaled")
        fold_added = sem("fold_added")
        w_loaded = [sem(f"w_loaded{b}") for b in range(2)]
        w_turned = sem("w_turned")
        w_rounded = sem("w_rounded")
        w_ready = sem("w_ready")
        x_loaded = [sem(f"x_loaded{b}") for b in range(2)]
        y_loaded = [sem(f"y_loaded{b}") for b in range(2)]
        x_turned = sem("x_turned")
        x_rounded = sem("x_rounded")
        x_ready = sem("x_ready")
        tile_done = sem("tile_done")
        moved = sem("moved")
        stored = [sem(f"stored{b}") for b in range(2)]
        bias_loaded = sem("bias_loaded")
        rest_loaded = [sem(f"rest_loaded{b}") for b in range(2)]
        rest_biased = sem("rest_biased")
        out_added = sem("out_added")
        out_stored = [sem(f"out_stored{b}") for b in range(2)]

        route_steps = []

        block = ctx.enter_context(nc.Block())

        def entry(eng, table, i, top):
            return eng.value_load(table[0:1, bass.ds(i, 1)], min_val=0, max_val=top)

        @block.sync
        def _(sp):
            def load_expert(k, src):
                for c in range(LOADS):
                    if not (isinstance(k, int) and k == 0 and c < 2):
                        sp.wait_ge(w_turned, k * CHUNKS + 2 * (c - 1))
                    rows = src[2 * c * P:2 * (c + 1) * P, :].rearrange("(m j) n -> j m n", j=BLK)
                    for q in range(QUADS):
                        sp.dma_start(w_raw[c % 2][BLK * q:BLK * (q + 1), :, :],
                                     rows[:, :, q * SEG:(q + 1) * SEG]).then_inc(w_loaded[c % 2], 16)

            def one(tensor, i):
                return tensor[bass.ds(i, 1)].rearrange("a s n -> (a s) n")

            def load_y(t, group, u):
                b = (SLOTS + u) % 2
                pos = [entry(sp, order_pos, 2 * t + h, POS - 1) for h in range(2)]
                last = [u + EXPERTS // 2 - (p if isinstance(group, int) else 0) for p in range(2)]
                stores = [sp.snap(group * (32 * RING // 2) + 16 * (FOLDS // 2) + 32 * (last[p] // 2 + 1))
                          for p in range(2)]
                turned = sp.snap(2 * (t + SLOTS) - 2)
                for p in range(2):
                    sp.wait_ge(stored[p], stores[p])
                sp.wait_ge(x_turned, turned)
                for h in range(2):
                    sp.dma_start(x_raw[b][:, 2 * h:2 * h + 2, :].rearrange("p m n -> p (m n)"),
                                 y_scr[bass.ds(pos[h], 1)].rearrange("a q (j m) n -> (a q j) (m n)", m=2)
                                 ).then_inc(y_loaded[b], 16)

            def load_rest(t, b, stores=None):
                samples = [entry(sp, order_sample, 2 * t + h, SAMPLES - 1) for h in range(2)]
                if stores is not None:
                    sp.wait_ge(out_stored[b], stores)
                for h in range(2):
                    sp.dma_start(stage[b][h * TOK:(h + 1) * TOK, :], one(x, samples[h])).then_inc(rest_loaded[b], 16)

            def load_next_expert(slot):
                opens = entry(sp, slot_opens, 2 * slot, 1)
                with sp.If(opens > 0):
                    rank = entry(sp, slot_rank, 2 * slot, EXPERTS - 1)
                    load_rank(rank + 1)
                with sp.Else():
                    sp.nop()

            def load_rank(k):
                e = entry(sp, rank_expert, k, EXPERTS)
                with sp.If(e < EXPERTS):
                    load_expert(k, one(w, entry(sp, rank_expert, k, EXPERTS - 1)))
                with sp.Else():
                    load_expert(k, weff)
                sp.nop()

            sp.dma_start(ids_i[:, :], ids.rearrange("(s a) -> s a", a=1)).then_inc(ids_loaded, 16)
            load_expert(0, w[0])
            sp.wait_ge(tables, 1)
            for p in range(2):
                sp.wait_ge(stored[p], 16 * (FOLDS // 2))
            load_rank(1)
            with sp.Fori(0, SLOTS - AHEAD) as slot:
                load_next_expert(slot)
            for u in range(AHEAD):
                load_y(u, 0, u)
                load_next_expert(SLOTS - AHEAD + u)
            load_y(AHEAD, 0, AHEAD)
            ranks = entry(sp, n_ranks, 0, EXPERTS)
            sp.wait_ge(w_turned, ranks * CHUNKS + CHUNKS)
            sp.dma_start(bias_sb, bias.rearrange("(a n) -> a n", a=1).to_broadcast([P, D])).then_inc(bias_loaded, 16)
            for t in range(2):
                sp.wait_ge(stored[t], 16 * (FOLDS // 2) + 32 * (SLOTS // 2))
                load_rest(t, t)

            def out_step(g, u, last):
                t = g * RING + u
                if not last:
                    load_y(t + RING, g + 1, u)
                if not (last and u + 2 >= RING):
                    load_rest(t + 2, u % 2, g * (32 * RING // 2) + 32 * (u // 2 + 1))

            with sp.Fori(0, TILES // RING - 1) as g:
                for u in range(RING):
                    out_step(g, u, False)
            for u in range(RING):
                out_step(TILES // RING - 1, u, True)
            for b in range(2):
                sp.wait_ge(out_stored[b], 32 * TILES // 2)

        @block.gpsimd
        def _(pool):
            nc.gpsimd.iota(iota_i[:, :], [[1, POS]], base=0, channel_multiplier=0).then_inc(iotas, 1)
            nc.gpsimd.iota(chan_i[:, :], [[0, 1]], base=0, channel_multiplier=1).then_inc(iotas, 1)

            def load_x(n, b):
                samples = [entry(pool, slot_sample, 2 * n + h, SAMPLES - 1) for h in range(2)]
                if not (isinstance(n, int) and n < 2):
                    pool.wait_ge(x_turned, 2 * n - 2)
                for h in range(2):
                    rows = x[bass.ds(samples[h], 1)].rearrange("a (j m) n -> (a j) m n", m=2)
                    for q in range(QUADS):
                        pool.dma_start(x_raw[b][BLK * q:BLK * (q + 1), 2 * h:2 * h + 2, :],
                                       rows[:, :, q * SEG:(q + 1) * SEG]).then_inc(x_loaded[b], 16)

            pool.wait_ge(tables, 1)
            for n in range(RING):
                load_x(n, n % 2)
            pool.wait_ge(base_loaded, 16)
            for f in range(FOLDS):
                pool.wait_ge(moved, f + 1)
                nc.gpsimd.tensor_tensor(fold_w[:, f, :], fold_w[:, f, :], stage[f % 2][:, :],
                                        ALU.add).then_inc(fold_added, 1)
            with pool.Fori(RING // 2, SLOTS // 2) as g:
                for b in range(2):
                    load_x(2 * g + b, b)
            pool.wait_ge(bias_loaded, 16)
            with pool.Fori(0, TILES // 2) as g:
                for b in range(2):
                    pool.wait_ge(rest_loaded[b], g * 32 + 32)
                    nc.gpsimd.tensor_tensor(stage[b][:, :], stage[b][:, :],
                                            bias_sb, ALU.add).then_inc(rest_biased, 1)

        @block.scalar
        def _(act):
            for n in range(NLORA):
                act.dma_start(b_sb[:, :, n, :], lora_b[n].rearrange("(f p) r -> p f r", p=P)).then_inc(lora_loaded, 16)
            act.dma_start(a_sb[:, :], lora_a.rearrange("n r d -> (n r) d")).then_inc(lora_loaded, 16)
            for n in range(NLORA):
                act.dma_start(coef[n * RANK:(n + 1) * RANK, :],
                              lora_weights[n:n + 1].rearrange("(a b) -> a b", a=1).to_broadcast([RANK, 1])
                              ).then_inc(lora_loaded, 16)
            act.dma_start(fold_w[:, :, :], base_w.rearrange("(f p) n -> p f n", p=P)).then_inc(base_loaded, 16)

            def round_w(k, par):
                for c in range(CHUNKS):
                    act.wait_ge(w_turned, k * CHUNKS + (c + 1))
                    dst = w_hi[:, bass.ds(par, 1), :, c * P:(c + 1) * P].rearrange("p a t m -> p (a t) m")
                    nc.scalar.activation(dst, w_turn[c % TURN][:, :, :], COPY).then_inc(w_rounded, 1)

            def round_x(n, b):
                if not (isinstance(n, int) and n < RING):
                    act.wait_ge(tile_done, n + (FOLDS - RING + 1))
                for h in range(2):
                    act.wait_ge(x_turned, 2 * n + (h + 1))
                    nc.scalar.activation(x_hi[b][:, h * KT // 2:(h + 1) * KT // 2, :],
                                         x_turn[h][:, :, :], COPY).then_inc(x_rounded, 1)

            def round_next_expert(slot):
                opens = entry(act, slot_opens, 2 * slot, 1)
                with act.If(opens > 0):
                    rank = entry(act, slot_rank, 2 * slot, EXPERTS - 1)
                    act.wait_ge(tile_done, slot + FOLDS)
                    round_w(rank + 1, (rank + 1) % 2)
                with act.Else():
                    act.nop()

            def move_y(slot, u, g):
                act.wait_ge(tile_done, slot + (FOLDS + 1))
                act.wait_ge(stored[u % 2], g * (32 * RING // 2) + (16 * (FOLDS // 2) + 32 * (u // 2)))
                nc.scalar.activation(stage[u % 2][:, :], ps[u][:, :], COPY).then_inc(moved, 1)
                act.wait_ge(moved, slot + (FOLDS + 1))
                for h in range(2):
                    act.dma_start(y_scr[bass.ds(2 * slot + h, 1)].rearrange("a q s n -> s (a q) n"),
                                  stage[u % 2][h * TOK:(h + 1) * TOK, :].rearrange("s (q n) -> s q n", q=QUADS)
                                  ).then_inc(stored[u % 2], 16)

            round_w(0, 0)
            act.wait_ge(tables, 1)
            for n in range(AHEAD):
                round_x(n, n)

            def store_fold(f):
                act.wait_ge(fold_added, f + 1)
                act.dma_start(weff[f * P:(f + 1) * P, :], fold_w[:, f, :]).then_inc(stored[f % 2], 16)

            for f in range(FOLDS):
                act.wait_ge(tile_done, f + 1)
                if f >= 2:
                    act.wait_ge(fold_added, f - 1)
                nc.scalar.activation(stage[f % 2][:, :], ps[f % RING][:, :], COPY).then_inc(moved, 1)
                if f >= 1:
                    store_fold(f - 1)
            store_fold(FOLDS - 1)
            for p in range(2):
                act.wait_ge(stored[p], 16 * (FOLDS // 2))
            round_w(1, 1)
            with act.Fori(0, SLOTS // RING) as g:
                for u in range(RING):
                    slot = g * RING + u
                    round_x(slot + AHEAD, (u + AHEAD) % RING)
                    round_next_expert(slot)
                    move_y(slot, u, g)

            def out_step(g, u, last):
                t = g * RING + u
                if not (last and u + AHEAD >= RING):
                    round_x(t + (SLOTS + AHEAD), (u + AHEAD) % RING)
                act.wait_ge(out_added, t + 1)
                for h in range(2):
                    s = entry(act, order_sample, 2 * t + h, SAMPLES - 1)
                    act.dma_start(out[bass.ds(s, 1)].rearrange("a s n -> (a s) n"),
                                  stage[u % 2][h * TOK:(h + 1) * TOK, :]).then_inc(out_stored[u % 2], 16)

            with act.Fori(0, TILES // RING - 1) as g:
                for u in range(RING):
                    out_step(g, u, False)
            for u in range(RING):
                out_step(TILES // RING - 1, u, True)

        @block.vector
        def _(dve):
            step = [0]

            def link(ins):
                step[0] += 1
                ins.then_inc(routing, 1)
                dve.wait_ge(routing, step[0])

            tt, tsc, cp = nc.vector.tensor_tensor, nc.vector.tensor_scalar, nc.vector.tensor_copy

            link(nc.vector.memset(ones[:, :], 1.0))
            dve.wait_ge(iotas, 2)
            link(cp(iota_f[:, :], iota_i[:, :]))
            link(cp(chan_f[:, :], chan_i[:, :]))
            dve.wait_ge(ids_loaded, 16)
            link(cp(ids_f[:, :], ids_i[:, :]))
            link(tsc(before[:, :], iota_f[:, 0:P], chan_f[:, 0:1], None, ALU.is_gt))
            link(tsc(ident[:, :], iota_f[:, 0:P], chan_f[:, 0:1], None, ALU.is_equal))
            link(tsc(onehot[:, :], iota_f[:, 0:EXPERTS], ids_f[:, 0:1], None, ALU.is_equal))
            onehot_step = step[0]
            dve.wait_ge(counted, 1)
            link(cp(counts[:, 2, :], ps[0][:, 0:EXPERTS]))
            link(cp(counts[:, 3, :], ps[0][:, EXPERTS:2 * EXPERTS]))
            link(tsc(counts[:, 1, :], counts[:, 2, :], 0.0, None, ALU.is_gt))
            link(nc.vector.memset(counts[:, 1, 0:1], 1.0))
            link(tsc(halves_i[:, :], counts[:, 2, :], 1.0, None, ALU.add))
            link(tsc(halves_i[:, :], halves_i[:, :], 1, None, ALU.arith_shift_right))
            link(cp(counts[:, 0, :], halves_i[:, :]))
            link(cp(scan[:, 0, :, :], counts[:, 0:3, :]))
            src, d = 0, 1
            while d < EXPERTS:
                link(cp(scan[:, 1 - src, :, 0:d], scan[:, src, :, 0:d]))
                link(tt(scan[:, 1 - src, :, d:], scan[:, src, :, d:], scan[:, src, :, :EXPERTS - d], ALU.add))
                src, d = 1 - src, 2 * d
            link(cp(n_ranks[0:1, :], scan[0:1, src, 1, EXPERTS - 1:EXPERTS]))
            link(tt(counts[:, 0:3, :], scan[:, src, :, :], counts[:, 0:3, :], ALU.subtract))
            for i in range(4):
                link(tt(picked[:, i, :], counts[:, i, :], onehot[:, :], ALU.mult))
            link(nc.vector.reduce_sum(mine[:, :], picked[:, :, :], AXX))
            link(cp(vals[:, 0:1], chan_f[:, :]))
            link(cp(vals[:, 1:2], mine[:, 1:2]))
            link(nc.vector.memset(vals[:, 3:4], 1.0))
            link(tsc(vals[:, 4:5], mine[:, 0:1], 2.0, mine[:, 3:4], ALU.mult, ALU.add))
            order = picked[:, 0, 0:1]
            link(tt(order, mine[:, 2:3], mine[:, 3:4], ALU.add))
            leads = picked[:, 1, 0:1]
            link(tsc(leads, mine[:, 3:4], 0.0, None, ALU.is_equal))
            link(tsc(vals[:, 2:3], mine[:, 1:2], 0.5, leads, ALU.is_gt, ALU.mult))
            link(tsc(vals[:, 5:6], ids_f[:, :], float(-EXPERTS), leads, ALU.add, ALU.mult))
            link(tsc(at_pos[:, :], iota_f[:, 0:POS], vals[:, 4:5], None, ALU.is_equal))
            link(tsc(at_order[:, :], iota_f[:, 0:SAMPLES], order, None, ALU.is_equal))
            link(tsc(at_rank[:, :], iota_f[:, 0:EXPERTS + 1], mine[:, 1:2], None, ALU.is_equal))
            listed_step = step[0]
            dve.wait_ge(listed, 1)
            link(cp(slot_sample[:, :], ps[1][0:1, 0:POS]))
            link(cp(slot_rank[:, :], ps[1][0:1, POS:2 * POS]))
            link(cp(slot_opens[:, :], ps[1][0:1, 2 * POS:3 * POS]))
            link(cp(slot_used[:, :], ps[1][0:1, HALF:HALF + POS]))
            link(cp(order_sample[:, :], ps[1][0:1, HALF + POS:HALF + POS + SAMPLES]))
            link(cp(order_pos[:, :], ps[1][0:1, HALF + POS + SAMPLES:HALF + POS + 2 * SAMPLES]))
            link(tsc(rank_expert[:, :], ps[2][0:1, 0:EXPERTS + 1], float(EXPERTS), None, ALU.add))
            nc.vector.memset(counts[:, 0, 0:1], 0.0).then_inc(tables, 1)

            def turn_w(k, c):
                load, part = c // 2, c % 2
                if part == 0:
                    dve.wait_ge(w_loaded[load % 2], 16 * QUADS * (load // 2 + 1) + k * (16 * QUADS * LOADS // 2))
                if not (isinstance(k, int) and k == 0 and c < TURN):
                    dve.wait_ge(w_ready, k * CHUNKS + (c - TURN + 1))
                nc.vector.transpose(w_turn[c % TURN][:, :, :].rearrange("p t (m j) -> p m t j", j=BLK),
                                    w_raw[load % 2][:, part * P // BLK:(part + 1) * P // BLK, :].rearrange("p m (t i) -> p m t i", i=BLK)
                                    ).then_inc(w_turned, 1)

            def split_w(k, par, c):
                dve.wait_ge(w_rounded, k * CHUNKS + (c + 1))
                part = slice(c * P, (c + 1) * P)
                hi = w_hi[:, bass.ds(par, 1), :, part].rearrange("p a t m -> p (a t) m")
                lo = w_lo[:, bass.ds(par, 1), :, part].rearrange("p a t m -> p (a t) m")
                tt(lo, w_turn[c % TURN][:, :, :], hi, ALU.subtract).then_inc(w_ready, 1)

            def scale_b():
                dve.wait_ge(b_turned, 1)
                tsc(bt_sb[:, :], ps[3][:, :], coef[:, 0:1], LORA_SCALE, ALU.mult, ALU.mult).then_inc(b_scaled, 1)

            def prepare_w(k, par):
                for c in range(CHUNKS):
                    if isinstance(k, int) and k == 0 and c == CHUNKS // 2:
                        scale_b()
                    turn_w(k, c)
                    if c:
                        split_w(k, par, c - 1)
                split_w(k, par, CHUNKS - 1)

            def prepare_x(n, b, raw, load, loaded=x_loaded, loads=2 * QUADS):
                dve.wait_ge(loaded[raw], load * (16 * loads) + 16 * loads)
                for h in range(2):
                    if not (isinstance(n, int) and n == 0):
                        dve.wait_ge(x_ready, 2 * n + (h - 1))
                    ts = slice(h * KT // 2 * BLK, (h + 1) * KT // 2 * BLK)
                    for s in range(2):
                        last = nc.vector.transpose(
                            x_turn[h][:, :, s * TOK:(s + 1) * TOK].rearrange("p t (j m) -> p m t j", m=2),
                            x_raw[raw][:, 2 * s:2 * s + 2, ts].rearrange("p m (t i) -> p m t i", i=BLK))
                    last.then_inc(x_turned, 1)
                for h in range(2):
                    dve.wait_ge(x_rounded, 2 * n + (h + 1))
                    ts = slice(h * KT // 2, (h + 1) * KT // 2)
                    tt(x_lo[b][:, ts, :], x_turn[h][:, :, :], x_hi[b][:, ts, :], ALU.subtract).then_inc(x_ready, 1)

            def prepare_next_expert(slot):
                opens = entry(dve, slot_opens, 2 * slot, 1)
                with dve.If(opens > 0):
                    rank = entry(dve, slot_rank, 2 * slot, EXPERTS - 1)
                    prepare_w(rank + 1, (rank + 1) % 2)
                with dve.Else():
                    dve.nop()

            prepare_w(0, 0)
            for n in range(AHEAD):
                prepare_x(n, n, n % 2, n // 2)
            prepare_w(1, 1)
            with dve.Fori(0, SLOTS // RING - 1) as g:
                for u in range(RING):
                    slot = g * RING + u
                    v = u + AHEAD
                    prepare_x(slot + AHEAD, v % RING, v % 2, g * (RING // 2) + v // 2)
                    prepare_next_expert(slot)
            for u in range(RING):
                slot = SLOTS - RING + u
                n = slot + AHEAD
                if n < SLOTS:
                    prepare_x(n, n % RING, n % 2, n // 2)
                else:
                    prepare_x(n, n % RING, n % 2, (n - SLOTS) // 2, y_loaded, 2)
                prepare_next_expert(slot)

            def out_step(g, u, last):
                t = g * RING + u
                v = u + AHEAD
                if not (last and v >= RING):
                    prepare_x(t + (SLOTS + AHEAD), v % RING, v % 2, g * (RING // 2) + v // 2, y_loaded, 2)
                dve.wait_ge(tile_done, t + (FOLDS + SLOTS + 1))
                dve.wait_ge(rest_biased, t + 1)
                tt(stage[u % 2][:, :], ps[u][:, :], stage[u % 2][:, :], ALU.add).then_inc(out_added, 1)

            with dve.Fori(0, TILES // RING - 1) as g:
                for u in range(RING):
                    out_step(g, u, False)
            for u in range(RING):
                out_step(TILES // RING - 1, u, True)
            route_steps[:] = [onehot_step, listed_step]

        @block.tensor
        def _(pe):
            mm = nc.tensor.matmul
            onehot_step, listed_step = route_steps
            pe.wait_ge(routing, onehot_step)
            mm(ps[0][:, 0:EXPERTS], ones[:, :], onehot[:, :], start=True, stop=True)
            mm(ps[0][:, EXPERTS:2 * EXPERTS], before[:, :], onehot[:, :], start=True, stop=True).then_inc(counted, 1)
            pe.wait_ge(routing, listed_step)
            mm(ps[1][0:1, 0:POS], vals[:, 0:1], at_pos[:, :], start=True, stop=True)
            mm(ps[1][0:1, POS:2 * POS], vals[:, 1:2], at_pos[:, :], start=True, stop=True)
            mm(ps[1][0:1, 2 * POS:3 * POS], vals[:, 2:3], at_pos[:, :], start=True, stop=True)
            mm(ps[1][0:1, HALF:HALF + POS], vals[:, 3:4], at_pos[:, :], start=True, stop=True)
            mm(ps[1][0:1, HALF + POS:HALF + POS + SAMPLES], vals[:, 0:1], at_order[:, :], start=True, stop=True)
            mm(ps[1][0:1, HALF + POS + SAMPLES:HALF + POS + 2 * SAMPLES], vals[:, 4:5], at_order[:, :],
               start=True, stop=True)
            mm(ps[2][0:1, 0:EXPERTS + 1], vals[:, 5:6], at_rank[:, :], start=True, stop=True).then_inc(listed, 1)
            pe.wait_ge(lora_loaded, 16 * (2 * NLORA + 1))
            for f in range(FOLDS):
                last = nc.tensor.transpose(ps[3][:, f * P:(f + 1) * P],
                                           b_sb[:, f, :, :].rearrange("p n r -> p (n r)"), ident[:, :])
            last.then_inc(b_turned, 1)
            pe.wait_ge(b_scaled, 1)
            pe.wait_ge(tables, 1)
            for f in range(FOLDS):
                if f >= RING:
                    pe.wait_ge(moved, f - RING + 1)
                for half in range(2):
                    cols = slice(half * HALF, (half + 1) * HALF)
                    last = mm(ps[f % RING][:, cols], bt_sb[:, f * P:(f + 1) * P], a_sb[:, cols],
                              start=True, stop=True)
                last.then_inc(tile_done, 1)

            def products(b, par, ready):
                for half in range(2):
                    pe.wait_ge(w_ready, ready + (half + 1) * CHUNKS // 2)
                    cols = slice(half * HALF, (half + 1) * HALF)
                    for t in range(KT):
                        hi = w_hi[:, bass.ds(par, 1), t, cols].rearrange("p a m -> p (a m)")
                        lo = w_lo[:, bass.ds(par, 1), t, cols].rearrange("p a m -> p (a m)")
                        mm(ps[b][:, cols], x_hi[b][:, t, :], hi, start=t == 0, stop=False)
                        mm(ps[b][:, cols], x_hi[b][:, t, :], lo, start=False, stop=False)
                        last = mm(ps[b][:, cols], x_lo[b][:, t, :], hi, start=False, stop=t == KT - 1)
                last.then_inc(tile_done, 1)

            with pe.Fori(0, SLOTS // RING) as g:
                for u in range(RING):
                    slot = g * RING + u
                    used = entry(pe, slot_used, 2 * slot, 1)
                    pe.wait_ge(x_ready, 2 * slot + 2)
                    pe.wait_ge(moved, slot + (FOLDS - RING + 1))
                    with pe.If(used > 0):
                        rank = entry(pe, slot_rank, 2 * slot, EXPERTS - 1)
                        products(u, rank % 2, rank * CHUNKS)
                    with pe.Else():
                        for half in range(2):
                            last = mm(ps[u][:, half * HALF:(half + 1) * HALF], x_hi[u][:, 0, :],
                                      x_hi[u][:, 0:KT // 2, :], start=True, stop=True)
                        last.then_inc(tile_done, 1)
            ranks = entry(pe, n_ranks, 0, EXPERTS)
            par = pe.snap(ranks % 2)
            ready = pe.snap(ranks * CHUNKS)
            for u in range(RING):
                pe.wait_ge(x_ready, 2 * (SLOTS + u) + 2)
                pe.wait_ge(moved, FOLDS + SLOTS - RING + u + 1)
                products(u, par, ready)
            with pe.Fori(1, TILES // RING) as g:
                for u in range(RING):
                    t = g * RING + u
                    pe.wait_ge(x_ready, 2 * t + (2 * SLOTS + 2))
                    pe.wait_ge(out_added, t - (RING - 1))
                    products(u, par, ready)


_INS = ['x', 'itok_B_0_15', 'L0_cond_weight', 'L0_ffn_lora_A', 'L0_ffn_lora_B', 'L0_ffn_W', 'L0_ffn_bias',
        'L0_ffn_lora_weights']
_OUTS = [((128, 64, 1024), 'float32')]


def kernel(**inputs):
    import numpy as _np
    import concourse.bacc as _bacc
    from concourse import mybir as _mybir
    from concourse.bass_utils import run_bass_kernel_spmd as _run

    nc = _bacc.Bacc("TRN2", target_bir_lowering=False, num_devices=1)
    arrays, args = {}, []
    for name in _INS:
        a = _np.ascontiguousarray(inputs[name])
        arrays[f"in_{name}_dram"] = a
        args.append(nc.dram_tensor(f"in_{name}_dram", a.shape, _mybir.dt.from_np(a.dtype), kind="ExternalInput").ap())
    for i, (shape, dtype) in enumerate(_OUTS):
        dt = _mybir.dt.from_np(_np.dtype(dtype))
        args.append(nc.dram_tensor(f"out_{i}_dram", shape, dt, kind="ExternalOutput").ap())
    grouped_adaln_ffn_kernel(nc, *args)
    r = _run(nc, [arrays], core_ids=[0])
    return r.results[0]["out_0_dram"]
```
